# Optimizing a Trainium2 kernel written in Bass

```python
import numpy as np
import jax
import jax.numpy as jnp

def _softmax(x, axis=-1):
    return jax.nn.softmax(x, axis=axis)

def _gelu(x):
    return jax.nn.gelu(x, approximate=True)

def _silu(x):
    return jax.nn.silu(x)

def _sigmoid(x):
    return jax.nn.sigmoid(x)

def _layernorm(x, axis=-1, eps=1e-05):
    m = jnp.mean(x, axis=axis, keepdims=True)
    v = jnp.var(x, axis=axis, keepdims=True)
    return (x - m) / jnp.sqrt(v + eps)

def _scatter_add(tgt, idx, src, axis=0):
    return tgt.at[idx].add(src)

def _segment_sum(src, seg, n):
    return jax.ops.segment_sum(src, seg, n)
kernel_name = 'mk_cond_resid_d1_seqx_r8_565f58'

def setup_inputs(seed: int=0):
    np.random.seed(seed)
    _w = jnp.asarray

    def _rec_inputs():
        import jax
        import jax.numpy as jnp
        _rk = jax.random.key(seed)
        x = -0.0003929 + 0.9999 * jax.random.normal(jax.random.fold_in(_rk, 1), (32, 128, 128), jnp.float32)
        _lenS = 128 - jax.random.randint(jax.random.fold_in(_rk, 7), (32,), 0, max(1, 128 // 4) + 1, jnp.int32)
        _lenS2 = 128 - jax.random.randint(jax.random.fold_in(_rk, 8), (32,), 0, max(1, 128 // 4) + 1, jnp.int32)
        itok_B_0_7 = jax.random.randint(jax.random.fold_in(_rk, 11), (32,), 0, 8, jnp.int32)
        return (x, itok_B_0_7)
    x, itok_B_0_7 = _rec_inputs()

    def _L0_cond_setup():
        import jax, jax.numpy as jnp
        import numpy as np
        B, S, D, F = (32, 64, 128, 512)
        R_COMMON, R_DOMAIN, E = (16, 16, 8)
        ALPHA = 2.0

        def _expert_lora(x, expert_ids, Wa, Wb):
            Ab = Wa[expert_ids]
            Bb = Wb[expert_ids]
            low = jnp.einsum('bsd,brd->bsr', x, Ab)
            return ALPHA * jnp.einsum('bsr,bor->bso', low, Bb)
        key = jax.random.key(seed)
        ks = jax.random.split(key, 12)
        sd = lambda k, shape: jax.random.normal(k, shape, dtype=jnp.float32) * (1.0 / np.sqrt(shape[-1]))
        return {'hidden_states': jax.random.normal(ks[0], (B, S, D), dtype=jnp.float32), 'expert_ids': jax.random.randint(ks[1], (B,), 0, E, dtype=jnp.int32), 'wi': sd(ks[2], (F, D)), 'wo': sd(ks[3], (D, F)), 'common_wi_a': sd(ks[4], (R_COMMON, D)), 'common_wi_b': sd(ks[5], (F, R_COMMON)), 'common_wo_a': sd(ks[6], (R_COMMON, F)), 'common_wo_b': sd(ks[7], (D, R_COMMON)), 'experts_wi_a': sd(ks[8], (E, R_DOMAIN, D)), 'experts_wi_b': sd(ks[9], (F, R_DOMAIN)) * jnp.ones((E, 1, 1)) * 0.0 + sd(ks[9], (E, F, R_DOMAIN)), 'experts_wo_a': sd(ks[10], (E, R_DOMAIN, F)), 'experts_wo_b': sd(ks[11], (E, D, R_DOMAIN))}
    _L0_cond_all = _L0_cond_setup()
    _L0_cond_in = {k: v for k, v in _L0_cond_all.items() if k in ('wi', 'wo', 'common_wi_a', 'common_wi_b', 'common_wo_a', 'common_wo_b', 'experts_wi_a', 'experts_wi_b', 'experts_wo_a', 'experts_wo_b')}
    del _L0_cond_all
    return {'x': x, 'itok_B_0_7': itok_B_0_7, 'L0_cond_wi': _L0_cond_in['wi'], 'L0_cond_wo': _L0_cond_in['wo'], 'L0_cond_common_wi_a': _L0_cond_in['common_wi_a'], 'L0_cond_common_wi_b': _L0_cond_in['common_wi_b'], 'L0_cond_common_wo_a': _L0_cond_in['common_wo_a'], 'L0_cond_common_wo_b': _L0_cond_in['common_wo_b'], 'L0_cond_experts_wi_a': _L0_cond_in['experts_wi_a'], 'L0_cond_experts_wi_b': _L0_cond_in['experts_wi_b'], 'L0_cond_experts_wo_a': _L0_cond_in['experts_wo_a'], 'L0_cond_experts_wo_b': _L0_cond_in['experts_wo_b']}

def reference(x, itok_B_0_7, L0_cond_wi, L0_cond_wo, L0_cond_common_wi_a, L0_cond_common_wi_b, L0_cond_common_wo_a, L0_cond_common_wo_b, L0_cond_experts_wi_a, L0_cond_experts_wi_b, L0_cond_experts_wo_a, L0_cond_experts_wo_b):
    import jax
    import jax.numpy as jnp

    def _L0_cond_ref(hidden_states, expert_ids, wi, wo, common_wi_a, common_wi_b, common_wo_a, common_wo_b, experts_wi_a, experts_wi_b, experts_wo_a, experts_wo_b):
        import jax, jax.numpy as jnp
        import numpy as np
        B, S, D, F = (32, 64, 128, 512)
        R_COMMON, R_DOMAIN, E = (16, 16, 8)
        ALPHA = 2.0

        def _expert_lora(x, expert_ids, Wa, Wb):
            Ab = Wa[expert_ids]
            Bb = Wb[expert_ids]
            low = jnp.einsum('bsd,brd->bsr', x, Ab)
            return ALPHA * jnp.einsum('bsr,bor->bso', low, Bb)
        x = hidden_states
        hidden_i = jnp.einsum('bsd,fd->bsf', x, wi)
        hidden_i += ALPHA * jnp.einsum('bsr,fr->bsf', jnp.einsum('bsd,rd->bsr', x, common_wi_a), common_wi_b)
        hidden_i += _expert_lora(x, expert_ids, experts_wi_a, experts_wi_b)
        hidden_i = jax.nn.relu(hidden_i)
        hidden_o = jnp.einsum('bsf,df->bsd', hidden_i, wo)
        hidden_o += ALPHA * jnp.einsum('bsr,dr->bsd', jnp.einsum('bsf,rf->bsr', hidden_i, common_wo_a), common_wo_b)
        hidden_o += _expert_lora(hidden_i, expert_ids, experts_wo_a, experts_wo_b)
        return hidden_o
    x = x + _L0_cond_ref(x, itok_B_0_7, L0_cond_wi, L0_cond_wo, L0_cond_common_wi_a, L0_cond_common_wi_b, L0_cond_common_wo_a, L0_cond_common_wo_b, L0_cond_experts_wi_a, L0_cond_experts_wi_b, L0_cond_experts_wo_a, L0_cond_experts_wo_b)
    return x

_drawn_inputs = setup_inputs


def setup_inputs(seed=0):
    import zlib

    import numpy as np

    out = dict(_drawn_inputs(seed))
    spreads = {}
    factors = {}
    for name, (base, spread) in spreads.items():
        noise = np.random.default_rng([zlib.crc32(name.encode()), seed]).standard_normal(out[name].shape)
        drawn = base * np.exp(spread * noise) if base else spread * noise
        out[name] = jnp.asarray(drawn.astype(out[name].dtype))
    for name, factor in factors.items():
        out[name] = (out[name] * factor).astype(out[name].dtype)
    return out
```

```python
import concourse.bass as bass
import concourse.mybir as mybir

B, S, D, F, R, E = 32, 128, 128, 512, 16, 8
ALPHA = 2.0
ROWS = 4
GROUPS = B // ROWS
PAIRS = ROWS // 2
TOK = ROWS * S
CH = F // 128
BLK = 4 * R

P_WI, P_EA, P_MASK, P_END = 0, F, F + E * R, F + E * R + 2
C_IA, C_IB, C_OA, C_OB, C_END = 0, D, D + F, D + 2 * F, 2 * D + 2 * F


def build(nc, x_t, x, ids, packed, common, ei_b, eo_a, eo_b, wo_t, out):
    F32, F32R, I32 = mybir.dt.float32, mybir.dt.float32r, mybir.dt.int32
    ALU, ACT = mybir.AluOpType, mybir.ActivationFunctionType

    from contextlib import ExitStack
    ctx = ExitStack()
    with ctx:
        def sb(name, shape, dt):
            return ctx.enter_context(nc.sbuf_tensor(name, shape, dt))

        def bank(name):
            return ctx.enter_context(nc.psum_tensor(name, [128, 512], F32))

        def sem(name):
            return ctx.enter_context(nc.semaphore(name))

        ids_sb = sb("ids_sb", [1, B], I32)
        xt_sb = sb("xt_sb", [128, GROUPS, TOK], F32)
        x_sb = sb("x_sb", [128, 2, GROUPS // 2, ROWS, D], F32)
        packed_sb = sb("packed_sb", [128, P_END], F32)
        common_sb = sb("common_sb", [R, C_END], F32)
        eo_a_sb = sb("eo_a_sb", [R, E, F], F32)
        eo_b_sb = sb("eo_b_sb", [R, E, D], F32)
        wo_sb = sb("wo_sb", [128, CH, D], F32)
        ei_b_raw = sb("ei_b_raw", [128, PAIRS, F], F32)

        w1 = sb("w1", [128, F], F32)
        w1_hi = sb("w1_hi", [128, F], F32R)
        w1_lo = sb("w1_lo", [128, F], F32R)
        wo_common = sb("wo_common", [128, CH, D], F32)
        w2 = sb("w2", [128, E, CH, D], F32)
        ea_blocks = sb("ea_blocks", [128, E, 2, BLK], F32R)
        pair_a = sb("pair_a", [128, PAIRS, 2, 2 * BLK], F32R)
        ei_b_hi = sb("ei_b_hi", [128, PAIRS, F], F32R)
        pair_b = sb("pair_b", [128, 2, PAIRS, F], F32R)

        x_hi = sb("x_hi", [128, 2, TOK], F32R)
        x_lo = sb("x_lo", [128, 2, TOK], F32R)
        low_hi = sb("low_hi", [128, TOK], F32R)
        low_blocks = sb("low_blocks", [128, 2, PAIRS, 2, S], F32R)
        hidden = sb("hidden", [128, 2, CH, TOK], F32)
        out_sb = sb("out_sb", [128, 2, ROWS, D], F32)

        up_ps = [bank(f"up_ps{c}") for c in range(CH)]
        low_ps = bank("low_ps")
        down_ps = [bank(f"down_ps{p}") for p in range(2)]
        fold_ps = bank("fold_ps")
        w2_ps = [down_ps[1], fold_ps, down_ps[0]]

        ids_in, common_in, packed_in = sem("ids_in"), sem("common_in"), sem("packed_in")
        x0_in, x1_in, xt_in = sem("x0_in"), sem("x1_in"), sem("xt_in")
        eo_in, wo_in = sem("eo_in"), sem("wo_in")
        ei_b_in = [sem(f"ei_b_in{q}") for q in range(PAIRS)]
        w1_product, wo_product, w2_product = sem("w1_product"), sem("wo_product"), sem("w2_product")
        low_product = sem("low_product")
        up_product = sem("up_product")
        down_product = sem("down_product")
        w1_hi_made, ea_hi_made = sem("w1_hi_made"), sem("ea_hi_made")
        x_hi_made = sem("x_hi_made")
        ei_b_hi_made = sem("ei_b_hi_made")
        low_hi_made = sem("low_hi_made")
        hidden_made = sem("hidden_made")
        w1_made, w1_lo_made, ea_made = sem("w1_made"), sem("w1_lo_made"), sem("ea_made")
        wo_common_made, w2_made = sem("wo_common_made"), sem("w2_made")
        x_lo_made = sem("x_lo_made")
        pair_a_made = sem("pair_a_made")
        pair_b_made = sem("pair_b_made")
        low_made = sem("low_made")
        out_made = sem("out_made")
        zeroed = sem("zeroed")
        out_slot = [sem(f"out_slot{p}") for p in range(2)]

        ea = packed_sb[:, P_EA:P_MASK].rearrange("p (e r) -> p e r", e=E)
        ea_blk = ea_blocks[:, :, :, :].rearrange("p e w (b r) -> p e (w b) r", r=R)
        neg_low_mask = packed_sb[:, P_MASK:P_MASK + 1]
        neg_b_mask = packed_sb[:, P_MASK + 1:P_MASK + 2]

        block = ctx.enter_context(nc.Block())

        @block.sync
        def _(sp):
            sp.dma_start(ids_sb[:, :], ids).then_inc(ids_in, 16)
            sp.dma_start(common_sb[:, :], common).then_inc(common_in, 16)
            sp.dma_start(packed_sb[:, :], packed).then_inc(packed_in, 16)

            def gather_ei_b(g, first=False):
                for r in range(ROWS):
                    q = r // 2
                    e = sp.value_load(ids_sb[0:1, bass.ds(g * ROWS + r, 1)], min_val=0, max_val=E - 1)
                    if not first and r % 2 == 0:
                        sp.wait_ge(pair_b_made, g * PAIRS - PAIRS + q + 1)
                    src = bass.AP(ei_b.tensor, e * (R * F), [[0, 4], [F, R], [1, F]])
                    at = BLK * (r % 2)
                    sp.dma_start(ei_b_raw[at:at + BLK, q, :], src).then_inc(ei_b_in[q], 16)

            def store(g, p):
                sp.wait_ge(out_made, g + 1)
                sp.dma_start(out[:, bass.ds(g, 1), :, :].rearrange("t g r d -> t (g r) d"),
                             out_sb[:, p, :, :]).then_inc(out_slot[p], 16)

            sp.wait_ge(ids_in, 16)
            gather_ei_b(0, first=True)
            gather_ei_b(1)
            with sp.Fori(0, (GROUPS - 2) // 2) as i:
                for k in range(2):
                    g = i * 2 + (k + 1)
                    gather_ei_b(g + 1)
                    store(g - 1, k)
            store(GROUPS - 2, 0)
            store(GROUPS - 1, 1)
            for p in range(2):
                sp.wait_ge(out_slot[p], 16 + 16 * (GROUPS // 2))

        @block.gpsimd
        def _(pool):
            pool.memset(ea_blk[:, :, 4:7, :].bitcast(F32), 0.0).then_inc(zeroed, 1)
            pool.memset(low_blocks[:, :, :, :, :].bitcast(F32), 0.0).then_inc(zeroed, 1)
            pool.dma_start(xt_sb[:, 2:GROUPS, :], x_t[:, 2:GROUPS, :]).then_inc(xt_in, 16)

        @block.scalar
        def _(act):
            act.dma_start(xt_sb[:, 0, :], x_t[:, 0, :]).then_inc(x0_in, 16)
            act.dma_start(eo_a_sb[:, :, :], eo_a).then_inc(eo_in, 16)
            act.dma_start(eo_b_sb[:, :, :], eo_b).then_inc(eo_in, 16)
            act.dma_start(wo_sb[:, :, :], wo_t).then_inc(wo_in, 16)
            act.dma_start(xt_sb[:, 1, :], x_t[:, 1, :]).then_inc(x1_in, 16)
            for p in range(2):
                act.dma_start(x_sb[:, p, :, :, :], x[:, p, :, :, :]).then_inc(out_slot[p], 16)

            def split_x(g, p, loaded):
                if loaded is xt_in:
                    act.wait_ge(up_product, g * CH - CH)
                act.wait_ge(loaded, 16)
                act.activation(x_hi[:, p, :], xt_sb[:, bass.ds(g, 1), :].rearrange("p g t -> p (g t)"),
                               ACT.Copy).then_inc(x_hi_made, 1)

            def split_ei_b(g, first=False):
                for q in range(PAIRS):
                    if not first:
                        act.wait_ge(pair_b_made, g * PAIRS - PAIRS + q + 1)
                    act.wait_ge(ei_b_in[q], g * 32 + 32)
                    act.activation(ei_b_hi[:, q, :], ei_b_raw[:, q, :], ACT.Copy).then_inc(ei_b_hi_made, 1)

            def split_low(g, first=False):
                if not first:
                    act.wait_ge(low_made, g * 2)
                act.wait_ge(low_product, g + 1)
                act.activation(low_hi[:, :], low_ps[:, :], ACT.Copy).then_inc(low_hi_made, 1)

            def relu(g, p, c):
                act.wait_ge(up_product, g * CH + c + 1)
                act.activation(hidden[:, p, c, :], up_ps[c][:, :], ACT.Relu).then_inc(hidden_made, 1)

            def group(g, p, loaded=None, prepare=True):
                if prepare:
                    split_x(g + 1, 1 - p, loaded)
                relu(g, p, 0)
                relu(g, p, 1)
                if prepare:
                    split_ei_b(g + 1)
                    split_low(g + 1)
                relu(g, p, 2)
                relu(g, p, 3)

            split_x(0, 0, x0_in)
            act.wait_ge(packed_in, 16)
            act.activation(ea_blk[:, :, 0:3, :],
                           ea.rearrange("p e (o r) -> p e o r", o=1).to_broadcast([128, E, 3, R]),
                           ACT.Copy, scale=ALPHA).then_inc(ea_hi_made, 1)
            act.activation(ea_blk[:, :, 7, :], ea, ACT.Copy, scale=ALPHA).then_inc(ea_hi_made, 1)
            act.wait_ge(w1_made, 1)
            act.activation(w1_hi[:, :], w1[:, :], ACT.Copy).then_inc(w1_hi_made, 1)
            split_low(0, first=True)
            split_ei_b(0, first=True)
            group(0, 0, x1_in)
            with act.Fori(0, (GROUPS - 2) // 2) as i:
                group(i * 2 + 1, 1, xt_in)
                group(i * 2 + 2, 0, xt_in)
            group(GROUPS - 1, 1, prepare=False)

        @block.vector
        def _(dve):
            def low_part_x(g, p):
                dve.wait_ge(x_hi_made, g + 1)
                dve.tensor_tensor(x_lo[:, p, :], xt_sb[:, bass.ds(g, 1), :].rearrange("p g t -> p (g t)"),
                                  x_hi[:, p, :], ALU.subtract).then_inc(x_lo_made, 1)

            def gather_ea(g, first=False):
                for r in range(ROWS):
                    e = dve.value_load(ids_sb[0:1, bass.ds(g * ROWS + r, 1)], min_val=0, max_val=E - 1)
                    if not first and r == 0:
                        dve.wait_ge(low_product, g)
                    dve.tensor_scalar(pair_a[:, r // 2, :, BLK * (r % 2):BLK * (r % 2) + BLK],
                                      ea_blocks[:, bass.ds(e, 1), :, :].rearrange("p e w c -> p (e w) c"),
                                      1.0, None, ALU.mult).then_inc(pair_a_made, 1)

            def blocks_b(g, p):
                for q in range(PAIRS):
                    dve.wait_ge(ei_b_hi_made, g * PAIRS + q + 1)
                    dve.scalar_tensor_tensor(out=pair_b[:, p, q, :], in0=ei_b_hi[:, q, :], scalar=neg_b_mask,
                                             in1=ei_b_raw[:, q, :], op0=ALU.mult, op1=ALU.add)\
                        .then_inc(pair_b_made, 1)

            def blocks_low(g, p):
                dve.wait_ge(low_hi_made, g + 1)
                for h in range(2):
                    at = slice(BLK * h, BLK * h + BLK)
                    dve.scalar_tensor_tensor(
                        out=low_blocks[at, p, :, h, :],
                        in0=low_hi[at, :].rearrange("p (q h t) -> p q h t", q=PAIRS, h=2)[:, :, h, :],
                        scalar=packed_sb[at, P_MASK:P_MASK + 1],
                        in1=low_ps[at, :].rearrange("p (q h t) -> p q h t", q=PAIRS, h=2)[:, :, h, :],
                        op0=ALU.mult, op1=ALU.add).then_inc(low_made, 1)

            def finish(i, p):
                g = i * 2 + p
                dve.wait_ge(out_slot[p], i * 16 + 16)
                dve.wait_ge(down_product, g + 1)
                dve.tensor_tensor(out_sb[:, p, :, :].rearrange("p r d -> p (r d)"), down_ps[p][:, :],
                                  x_sb[:, p, bass.ds(i, 1), :, :].rearrange("p i r d -> p (i r d)"), ALU.add)\
                    .then_inc(out_made, 1)

            def add_w2(e):
                dve.wait_ge(w2_product, e + 1)
                dve.scalar_tensor_tensor(out=w2[:, e, :, :].rearrange("p c d -> p (c d)"),
                                         in0=w2_ps[e % 3][:, :], scalar=ALPHA,
                                         in1=wo_common[:, :, :].rearrange("p c d -> p (c d)"),
                                         op0=ALU.mult, op1=ALU.add).then_inc(w2_made, 1)

            def group(g, p, i):
                low_part_x(g + 1, 1 - p)
                gather_ea(g + 1)
                blocks_b(g + 1, 1 - p)
                blocks_low(g + 1, 1 - p)
                finish(i, 1 - p)

            dve.wait_ge(packed_in, 16)
            dve.wait_ge(w1_product, 1)
            dve.scalar_tensor_tensor(out=w1[:, :], in0=fold_ps[:, :], scalar=ALPHA, in1=packed_sb[:, P_WI:P_EA],
                                     op0=ALU.mult, op1=ALU.add).then_inc(w1_made, 1)
            dve.wait_ge(ea_hi_made, 1)
            dve.scalar_tensor_tensor(out=ea_blk[:, :, 3, :], in0=ea, scalar=ALPHA, in1=ea_blk[:, :, 0, :],
                                     op0=ALU.mult, op1=ALU.subtract).then_inc(ea_made, 1)
            dve.wait_ge(ea_hi_made, 2)
            dve.wait_ge(zeroed, 1)
            dve.wait_ge(ea_made, 1)
            dve.wait_ge(ids_in, 16)
            gather_ea(0, first=True)
            low_part_x(0, 0)
            dve.wait_ge(w1_hi_made, 1)
            dve.tensor_tensor(w1_lo[:, :], w1[:, :], w1_hi[:, :], ALU.subtract).then_inc(w1_lo_made, 1)
            dve.wait_ge(zeroed, 2)
            blocks_low(0, 0)
            blocks_b(0, 0)
            dve.wait_ge(wo_in, 16)
            dve.wait_ge(wo_product, 1)
            dve.scalar_tensor_tensor(out=wo_common[:, :, :].rearrange("p c d -> p (c d)"), in0=down_ps[0][:, :],
                                     scalar=ALPHA, in1=wo_sb[:, :, :].rearrange("p c d -> p (c d)"),
                                     op0=ALU.mult, op1=ALU.add).then_inc(wo_common_made, 1)
            dve.wait_ge(wo_common_made, 1)
            add_w2(0)
            add_w2(1)
            add_w2(2)
            low_part_x(1, 1)
            gather_ea(1)
            add_w2(3)
            add_w2(4)
            blocks_b(1, 1)
            blocks_low(1, 1)
            for e in range(5, E):
                add_w2(e)
            with dve.Fori(0, (GROUPS - 2) // 2) as i:
                group(i * 2 + 1, 1, i)
                group(i * 2 + 2, 0, i)
            finish(GROUPS // 2 - 1, 0)
            finish(GROUPS // 2 - 1, 1)

        @block.tensor
        def _(pe):
            def fold_w2(e):
                if e == 1:
                    pe.wait_ge(w1_made, 1)
                elif e == 2:
                    pe.wait_ge(wo_common_made, 1)
                elif e >= 3:
                    pe.wait_ge(w2_made, e - 2)
                for c in range(CH):
                    last = pe.matmul(w2_ps[e % 3][:, c * D:(c + 1) * D], eo_a_sb[:, e, c * 128:(c + 1) * 128],
                                     eo_b_sb[:, e, :], start=True, stop=True)
                last.then_inc(w2_product, 1)

            def low(g, p, first=False):
                if not first:
                    pe.wait_ge(low_made, g * 2)
                pe.wait_ge(pair_a_made, (g + 1) * ROWS)
                pe.wait_ge(x_lo_made, g + 1)
                for q in range(PAIRS):
                    cols = slice(q * 2 * S, (q + 1) * 2 * S)
                    pe.matmul(low_ps[:, cols], pair_a[:, q, 0, :], x_hi[:, p, cols], start=True, stop=False)
                    last = pe.matmul(low_ps[:, cols], pair_a[:, q, 1, :], x_lo[:, p, cols], start=False, stop=True)
                last.then_inc(low_product, 1)

            def up(g, p, c, first=False):
                if not first:
                    pe.wait_ge(hidden_made, g * CH - CH + c + 1)
                cw = slice(c * 128, (c + 1) * 128)
                pe.matmul(up_ps[c][:, :], w1_hi[:, cw], x_hi[:, p, :], start=True, stop=False)
                pe.matmul(up_ps[c][:, :], w1_hi[:, cw], x_lo[:, p, :], start=False, stop=False)
                pe.matmul(up_ps[c][:, :], w1_lo[:, cw], x_hi[:, p, :], start=False, stop=False)
                if c == 0:
                    pe.wait_ge(low_made, g * 2 + 2)
                    pe.wait_ge(pair_b_made, (g + 1) * PAIRS)
                for q in range(PAIRS):
                    last = pe.matmul(up_ps[c][:, q * 2 * S:(q + 1) * 2 * S], pair_b[:, p, q, cw],
                                     low_blocks[:, p, q, :, :].rearrange("p h t -> p (h t)"),
                                     start=False, stop=(q == PAIRS - 1))
                last.then_inc(up_product, 1)

            def down(g, p, r):
                e = pe.value_load(ids_sb[0:1, bass.ds(g * ROWS + r, 1)], min_val=0, max_val=E - 1)
                if r == 0:
                    pe.wait_ge(hidden_made, (g + 1) * CH)
                for c in range(CH):
                    last = pe.matmul(down_ps[p][:, r * D:(r + 1) * D], hidden[:, p, c, r * S:(r + 1) * S],
                                     w2[:, bass.ds(e, 1), c, :].rearrange("p e d -> p (e d)"),
                                     start=(c == 0), stop=(c == CH - 1))
                if r == ROWS - 1:
                    last.then_inc(down_product, 1)

            def group(g, p, prepare=True):
                for j in range(ROWS):
                    up(g, p, j)
                    down(g - 1, 1 - p, j)
                    if j == 1 and prepare:
                        low(g + 1, 1 - p)

            pe.wait_ge(common_in, 16)
            pe.matmul(fold_ps[:, :], common_sb[:, C_IA:C_IB], common_sb[:, C_IB:C_OA], start=True, stop=True)\
                .then_inc(w1_product, 1)
            for c in range(CH):
                last = pe.matmul(down_ps[0][:, c * D:(c + 1) * D], common_sb[:, C_OA + c * 128:C_OA + (c + 1) * 128],
                                 common_sb[:, C_OB:C_END], start=True, stop=True)
            last.then_inc(wo_product, 1)
            low(0, 0, first=True)
            pe.wait_ge(eo_in, 32)
            fold_w2(0)
            pe.wait_ge(w1_lo_made, 1)
            pe.wait_ge(ids_in, 16)
            up(0, 0, 0, first=True)
            fold_w2(1)
            fold_w2(2)
            up(0, 0, 1, first=True)
            fold_w2(3)
            fold_w2(4)
            low(1, 1)
            up(0, 0, 2, first=True)
            fold_w2(5)
            fold_w2(6)
            up(0, 0, 3, first=True)
            fold_w2(7)
            pe.wait_ge(w2_made, E)
            with pe.Fori(0, (GROUPS - 2) // 2) as i:
                group(i * 2 + 1, 1)
                group(i * 2 + 2, 0)
            group(GROUPS - 1, 1, prepare=False)
            pe.wait_ge(out_made, GROUPS - 2)
            for r in range(ROWS):
                down(GROUPS - 1, 1, r)


def kernel(x, itok_B_0_7, L0_cond_wi, L0_cond_wo, L0_cond_common_wi_a, L0_cond_common_wi_b,
           L0_cond_common_wo_a, L0_cond_common_wo_b, L0_cond_experts_wi_a, L0_cond_experts_wi_b,
           L0_cond_experts_wo_a, L0_cond_experts_wo_b):
    import numpy as np
    import concourse.bacc as bacc
    from concourse.bass_utils import run_bass_kernel_spmd

    def lay(a):
        return np.ascontiguousarray(a)

    x = np.asarray(x)
    row = np.arange(128) % BLK // R
    masks = np.stack([np.where(row == 1, -1.0, 0.0), np.where(row == 2, -1.0, 0.0)], 1).astype(np.float32)
    ei_a = np.asarray(L0_cond_experts_wi_a).reshape(E * R, D)
    eo_a, eo_b = np.asarray(L0_cond_experts_wo_a), np.asarray(L0_cond_experts_wo_b)
    arrays = {
        "x_t": lay(x.reshape(B * S, D).T).reshape(D, GROUPS, TOK),
        "x": lay(x.reshape(GROUPS // 2, 2, ROWS, S, D).transpose(3, 1, 0, 2, 4)),
        "ids": lay(np.asarray(itok_B_0_7).reshape(1, B)),
        "packed": lay(np.concatenate([np.asarray(L0_cond_wi).T, ei_a.T, masks], 1)),
        "common": lay(np.concatenate([np.asarray(L0_cond_common_wi_a), np.asarray(L0_cond_common_wi_b).T,
                                      np.asarray(L0_cond_common_wo_a), np.asarray(L0_cond_common_wo_b).T], 1)),
        "ei_b": lay(np.asarray(L0_cond_experts_wi_b).transpose(0, 2, 1)),
        "eo_a": lay(eo_a.transpose(1, 0, 2)),
        "eo_b": lay(eo_b.transpose(2, 0, 1)),
        "wo_t": lay(np.asarray(L0_cond_wo).T.reshape(CH, 128, D).transpose(1, 0, 2)),
    }
    nc = bacc.Bacc("TRN2", target_bir_lowering=False, num_devices=1)
    args = [nc.dram_tensor(n, a.shape, mybir.dt.from_np(a.dtype), kind="ExternalInput").ap()
            for n, a in arrays.items()]
    args.append(nc.dram_tensor("out", (S, GROUPS, ROWS, D), mybir.dt.float32, kind="ExternalOutput").ap())
    build(nc, *args)
    result = run_bass_kernel_spmd(nc, [arrays], core_ids=[0])
    return lay(result.results[0]["out"].reshape(S, B, D).transpose(1, 0, 2))
```

```python
import concourse.bass as bass
import concourse.mybir as mybir

B, S, D, F, R, E = 32, 128, 128, 512, 16, 8
ALPHA = 2.0
ROWS = 4
GROUPS = B // ROWS
PAIRS = ROWS // 2
TOK = ROWS * S
CH = F // 128
BLK = 4 * R
EPAIRS = E // 2
FOLD = 3 * 2 * R
FOLDS = 2 * CH
WARM_UP = 6

P_WI, P_EA, P_MASK, P_END = 0, F, F + E * R, F + E * R + 4
C_IA, C_IB, C_OA, C_OB, C_END = 0, D, D + F, D + 2 * F, 2 * D + 2 * F


def build(nc, x_t, x, ids, packed, common, ei_b, eo_a, eo_b, wo_t, out):
    F32, F32R, I32 = mybir.dt.float32, mybir.dt.float32r, mybir.dt.int32
    ALU, ACT = mybir.AluOpType, mybir.ActivationFunctionType

    from contextlib import ExitStack
    ctx = ExitStack()
    with ctx:
        def sb(name, shape, dt):
            return ctx.enter_context(nc.sbuf_tensor(name, shape, dt))

        def bank(name):
            return ctx.enter_context(nc.psum_tensor(name, [128, 512], F32))

        def sem(name):
            return ctx.enter_context(nc.semaphore(name))

        ids_sb = sb("ids_sb", [1, B], I32)
        xt_sb = sb("xt_sb", [128, GROUPS, TOK], F32)
        x_sb = sb("x_sb", [128, 2, GROUPS // 2, ROWS, D], F32)
        packed_sb = sb("packed_sb", [128, P_END], F32)
        common_sb = sb("common_sb", [R, C_END], F32)
        eo_a_sb = sb("eo_a_sb", [FOLD, EPAIRS, F], F32)
        eo_b_sb = sb("eo_b_sb", [FOLD, EPAIRS, 2, D], F32)
        wo_sb = sb("wo_sb", [128, CH, D], F32)
        ei_b_raw = sb("ei_b_raw", [128, 2, PAIRS, F], F32)

        w1 = sb("w1", [128, F], F32)
        w1_hi = sb("w1_hi", [128, F], F32R)
        w1_lo = sb("w1_lo", [128, F], F32R)
        wo_common = sb("wo_common", [128, CH, D], F32)
        eo_a_hi = sb("eo_a_hi", [FOLD, EPAIRS, F], F32R)
        eo_b_hi = sb("eo_b_hi", [FOLD, EPAIRS, 2, D], F32R)
        fold_a = sb("fold_a", [FOLD, EPAIRS, F], F32R)
        fold_b = sb("fold_b", [FOLD, EPAIRS, 2, D], F32R)
        w2 = sb("w2", [128, E, CH, D], F32)
        ea_blocks = sb("ea_blocks", [128, E, 2, R, 4], F32R)
        pair_a = sb("pair_a", [128, 2, PAIRS, 2, 2 * BLK], F32R)
        ei_b_hi = sb("ei_b_hi", [128, PAIRS, F], F32R)
        pair_b = sb("pair_b", [128, 2, PAIRS, F], F32R)

        zeros = sb("zeros", [128, 512], F32R)

        x_hi = sb("x_hi", [128, 2, TOK], F32R)
        x_lo = sb("x_lo", [128, 2, TOK], F32R)
        low_hi = sb("low_hi", [128, TOK], F32R)
        low_blocks = sb("low_blocks", [128, 2, PAIRS, 2, S], F32R)
        hidden = sb("hidden", [128, 2, CH, TOK], F32)
        out_sb = sb("out_sb", [128, 2, ROWS, D], F32)

        up_ps = [bank(f"up_ps{c}") for c in range(CH)]
        low_ps = bank("low_ps")
        down_ps = [bank(f"down_ps{p}") for p in range(2)]
        fold_ps = bank("fold_ps")
        w1_ps = [down_ps[1], fold_ps]
        w2_ps = [down_ps[1], fold_ps, down_ps[0]]

        ids_in, common_in, packed_in = sem("ids_in"), sem("common_in"), sem("packed_in")
        x0_in, x1_in, xt_in = sem("x0_in"), sem("x1_in"), sem("xt_in")
        eo_a_in, eo_b_in, wo_in = sem("eo_a_in"), sem("eo_b_in"), sem("wo_in")
        ei_b_in = [[sem(f"ei_b_in{p}{q}") for q in range(PAIRS)] for p in range(2)]
        w1_product, wo_product, w2_product = sem("w1_product"), sem("wo_product"), sem("w2_product")
        low_product = sem("low_product")
        up_product = sem("up_product")
        down_product = sem("down_product")
        w1_hi_made, ea_hi_made, eo_hi_made = sem("w1_hi_made"), sem("ea_hi_made"), sem("eo_hi_made")
        x_hi_made = sem("x_hi_made")
        ei_b_hi_made = sem("ei_b_hi_made")
        low_hi_made = sem("low_hi_made")
        hidden_made = sem("hidden_made")
        w1_made, w1_lo_made, ea_made = sem("w1_made"), sem("w1_lo_made"), sem("ea_made")
        wo_common_made, w2_made = sem("wo_common_made"), sem("w2_made")
        fold_a_made, fold_b_made = sem("fold_a_made"), sem("fold_b_made")
        x_lo_made = sem("x_lo_made")
        pair_a_made = sem("pair_a_made")
        pair_b_made = sem("pair_b_made")
        low_made = sem("low_made")
        out_made = sem("out_made")
        zeroed = sem("zeroed")
        out_slot = [sem(f"out_slot{p}") for p in range(2)]

        ea = packed_sb[:, P_EA:P_MASK].rearrange("p (e r) -> p e r", e=E)

        def minus_one_on(k, rows=slice(0, 128)):
            return packed_sb[rows, P_MASK + k:P_MASK + k + 1]

        P1_LOW, B_LOW, FOLD_A_LOW, FOLD_B_LOW = range(4)

        block = ctx.enter_context(nc.Block())

        @block.sync
        def _(sp):
            sp.dma_start(common_sb[:, :], common).then_inc(common_in, 16)
            sp.dma_start(ids_sb[:, :], ids).then_inc(ids_in, 16)

            def gather_ei_b(g, p):
                for r in range(ROWS):
                    q = r // 2
                    e = sp.value_load(ids_sb[0:1, bass.ds(g * ROWS + r, 1)], min_val=0, max_val=E - 1)
                    src = bass.AP(ei_b.tensor, e * (R * F), [[F, R], [0, 4], [1, F]])
                    at = BLK * (r % 2)
                    sp.dma_start(ei_b_raw[at:at + BLK, p, q, :], src).then_inc(ei_b_in[p][q], 16)

            def store(g, p):
                sp.wait_ge(out_made, g + 1)
                sp.dma_start(out[:, bass.ds(g, 1), :, :].rearrange("t g r d -> t (g r) d"),
                             out_sb[:, p, :, :]).then_inc(out_slot[p], 16)

            sp.wait_ge(ids_in, 16)
            gather_ei_b(0, 0)
            gather_ei_b(1, 1)
            sp.wait_ge(wo_in, 16)
            for p in range(2):
                sp.dma_start(x_sb[:, p, :, :, :], x[:, p, :, :, :]).then_inc(out_slot[p], 16)
            sp.wait_ge(pair_b_made, PAIRS)
            gather_ei_b(2, 0)
            with sp.Fori(0, (GROUPS - 4) // 2) as i:
                for k in range(2):
                    g = i * 2 + (k + 3)
                    sp.wait_ge(pair_b_made, g * PAIRS - PAIRS)
                    gather_ei_b(g, 1 - k)
                    store(g - 3, k)
            sp.wait_ge(pair_b_made, (GROUPS - 2) * PAIRS)
            gather_ei_b(GROUPS - 1, 1)
            for g in range(GROUPS - 4, GROUPS):
                store(g, g % 2)
            for p in range(2):
                sp.wait_ge(out_slot[p], 16 + 16 * (GROUPS // 2))

        @block.gpsimd
        def _(pool):
            pool.memset(zeros[:, :].bitcast(F32), 0.0).then_inc(zeroed, 1)
            pool.dma_start(eo_b_sb[:, :, :, :].rearrange("p a e d -> p (a e d)"),
                           bass.AP(eo_b.tensor, 0, [[EPAIRS * 2 * D, 2 * R], [0, 3], [1, EPAIRS * 2 * D]]))\
                .then_inc(eo_b_in, 16)
            pool.dma_start(eo_a_sb[:, :, :].rearrange("p a f -> p (a f)"),
                           bass.AP(eo_a.tensor, 0, [[EPAIRS * F, 2 * R], [0, 3], [1, EPAIRS * F]]))\
                .then_inc(eo_a_in, 16)
            pool.dma_start(wo_sb[:, :, :], wo_t).then_inc(wo_in, 16)
            pool.memset(ea_blocks[:, :, 1, :, 0:3].bitcast(F32), 0.0).then_inc(zeroed, 1)
            pool.memset(low_blocks[:, :, :, :, :].bitcast(F32), 0.0).then_inc(zeroed, 1)

            def gather_ea(g, p):
                for r in range(ROWS):
                    e = pool.value_load(ids_sb[0:1, bass.ds(g * ROWS + r, 1)], min_val=0, max_val=E - 1)
                    pool.tensor_copy(pair_a[:, p, r // 2, :, BLK * (r % 2):BLK * (r % 2) + BLK],
                                     ea_blocks[:, bass.ds(e, 1), :, :, :].rearrange("p e w r b -> p (e w) (r b)"))\
                        .then_inc(pair_a_made, 1)

            pool.wait_ge(ids_in, 16)
            pool.wait_ge(zeroed, 3)
            pool.wait_ge(ea_hi_made, 2)
            pool.wait_ge(ea_made, 1)
            gather_ea(0, 0)
            gather_ea(1, 1)
            pool.wait_ge(wo_in, 16)
            pool.dma_start(xt_sb[:, 2:GROUPS, :], x_t[:, 2:GROUPS, :]).then_inc(xt_in, 16)
            with pool.Fori(0, (GROUPS - 2) // 2) as i:
                for k in range(2):
                    g = i * 2 + (k + 2)
                    pool.wait_ge(low_product, g - 1)
                    gather_ea(g, k)

        @block.scalar
        def _(act):
            act.dma_start(packed_sb[:, :], packed).then_inc(packed_in, 16)
            act.dma_start(xt_sb[:, 0, :], x_t[:, 0, :]).then_inc(x0_in, 16)
            act.dma_start(xt_sb[:, 1, :], x_t[:, 1, :]).then_inc(x1_in, 16)

            def split_x(g, p, loaded):
                if loaded is xt_in:
                    act.wait_ge(up_product, g * CH - CH)
                act.wait_ge(loaded, 16)
                act.activation(x_hi[:, p, :], xt_sb[:, bass.ds(g, 1), :].rearrange("p g t -> p (g t)"),
                               ACT.Copy).then_inc(x_hi_made, 1)

            def split_ei_b(g, p, nth, first=False):
                for q in range(PAIRS):
                    if not first:
                        act.wait_ge(pair_b_made, g * PAIRS - PAIRS + q + 1)
                    act.wait_ge(ei_b_in[p][q], nth * 32)
                    act.activation(ei_b_hi[:, q, :], ei_b_raw[:, p, q, :], ACT.Copy).then_inc(ei_b_hi_made, 1)

            def split_low(g, first=False):
                if not first:
                    act.wait_ge(low_made, g * 2)
                act.wait_ge(low_product, g + 1)
                act.activation(low_hi[:, :], low_ps[:, :], ACT.Copy).then_inc(low_hi_made, 1)

            def relu(g, p, c):
                act.wait_ge(up_product, g * CH + c + 1)
                act.activation(hidden[:, p, c, :], up_ps[c][:, :], ACT.Relu).then_inc(hidden_made, 1)

            def group(g, p, nth=None, loaded=None, prepare=True):
                if prepare:
                    split_x(g + 1, 1 - p, loaded)
                relu(g, p, 0)
                relu(g, p, 1)
                if prepare:
                    split_ei_b(g + 1, 1 - p, nth)
                    split_low(g + 1)
                relu(g, p, 2)
                relu(g, p, 3)

            act.wait_ge(packed_in, 16)
            act.activation(ea_blocks[:, :, 0, :, 0:3],
                           ea.rearrange("p e (r o) -> p e r o", o=1).to_broadcast([128, E, R, 3]),
                           ACT.Copy, scale=ALPHA).then_inc(ea_hi_made, 1)
            act.activation(ea_blocks[:, :, 1, :, 3], ea, ACT.Copy, scale=ALPHA).then_inc(ea_hi_made, 1)
            split_x(0, 0, x0_in)
            for h in range(2):
                act.wait_ge(w1_made, h + 1)
                act.activation(w1_hi[:, h * F // 2:(h + 1) * F // 2], w1[:, h * F // 2:(h + 1) * F // 2],
                               ACT.Copy).then_inc(w1_hi_made, 1)
            act.wait_ge(eo_b_in, 16)
            act.activation(eo_b_hi[:, :, :, :], eo_b_sb[:, :, :, :], ACT.Copy).then_inc(eo_hi_made, 1)
            split_ei_b(0, 0, 1, first=True)
            act.wait_ge(eo_a_in, 16)
            act.activation(eo_a_hi[:, :, 0:F // 2], eo_a_sb[:, :, 0:F // 2], ACT.Copy).then_inc(eo_hi_made, 1)
            split_low(0, first=True)
            act.activation(eo_a_hi[:, :, F // 2:F], eo_a_sb[:, :, F // 2:F], ACT.Copy).then_inc(eo_hi_made, 1)
            group(0, 0, 1, x1_in)
            with act.Fori(0, (GROUPS - 2) // 2) as i:
                group(i * 2 + 1, 1, i + 2, xt_in)
                group(i * 2 + 2, 0, i + 2, xt_in)
            group(GROUPS - 1, 1, prepare=False)

        @block.vector
        def _(dve):
            def low_part_x(g, p):
                dve.wait_ge(x_hi_made, g + 1)
                dve.tensor_tensor(x_lo[:, p, :], xt_sb[:, bass.ds(g, 1), :].rearrange("p g t -> p (g t)"),
                                  x_hi[:, p, :], ALU.subtract).then_inc(x_lo_made, 1)

            def blocks_b(g, p):
                for q in range(PAIRS):
                    dve.wait_ge(ei_b_hi_made, g * PAIRS + q + 1)
                    dve.scalar_tensor_tensor(out=pair_b[:, p, q, :], in0=ei_b_hi[:, q, :], scalar=minus_one_on(B_LOW),
                                             in1=ei_b_raw[:, p, q, :], op0=ALU.mult, op1=ALU.add)\
                        .then_inc(pair_b_made, 1)

            def blocks_low(g, p):
                dve.wait_ge(low_hi_made, g + 1)
                for h in range(2):
                    at = slice(BLK * h, BLK * h + BLK)
                    dve.scalar_tensor_tensor(
                        out=low_blocks[at, p, :, h, :],
                        in0=low_hi[at, :].rearrange("p (q h t) -> p q h t", q=PAIRS, h=2)[:, :, h, :],
                        scalar=minus_one_on(P1_LOW, at),
                        in1=low_ps[at, :].rearrange("p (q h t) -> p q h t", q=PAIRS, h=2)[:, :, h, :],
                        op0=ALU.mult, op1=ALU.add).then_inc(low_made, 1)

            def finish(i, p):
                g = i * 2 + p
                dve.wait_ge(out_slot[p], i * 16 + 16)
                dve.wait_ge(down_product, g + 1)
                dve.tensor_tensor(out_sb[:, p, :, :].rearrange("p r d -> p (r d)"), down_ps[p][:, :],
                                  x_sb[:, p, bass.ds(i, 1), :, :].rearrange("p i r d -> p (i r d)"), ALU.add)\
                    .then_inc(out_made, 1)

            def fold_a_half(h):
                cols = slice(h * F // 2, (h + 1) * F // 2)
                dve.wait_ge(eo_hi_made, h + 2)
                dve.scalar_tensor_tensor(out=fold_a[:, :, cols], in0=eo_a_hi[:, :, cols],
                                         scalar=minus_one_on(FOLD_A_LOW, slice(0, FOLD)), in1=eo_a_sb[:, :, cols],
                                         op0=ALU.mult, op1=ALU.add).then_inc(fold_a_made, 1)

            def add_w2(n):
                c, e = n // 2, n % 2 * 4
                dve.wait_ge(w2_product, n + 1)
                dve.scalar_tensor_tensor(
                    out=w2[:, e:e + 4, c, :], in0=w2_ps[n % 3][:, :].rearrange("p (e d) -> p e d", e=4), scalar=ALPHA,
                    in1=wo_common[:, c, :].rearrange("p (o d) -> p o d", o=1).to_broadcast([128, 4, D]),
                    op0=ALU.mult, op1=ALU.add).then_inc(w2_made, 1)

            def group(g, p, i):
                low_part_x(g + 1, 1 - p)
                blocks_b(g + 1, 1 - p)
                blocks_low(g + 1, 1 - p)
                finish(i, 1 - p)

            dve.wait_ge(packed_in, 16)
            for h in range(2):
                dve.wait_ge(w1_product, h + 1)
                dve.scalar_tensor_tensor(out=w1[:, h * F // 2:(h + 1) * F // 2], in0=w1_ps[h][:, 0:F // 2], scalar=ALPHA,
                                         in1=packed_sb[:, P_WI + h * F // 2:P_WI + (h + 1) * F // 2],
                                         op0=ALU.mult, op1=ALU.add).then_inc(w1_made, 1)
            dve.wait_ge(ea_hi_made, 1)
            dve.scalar_tensor_tensor(out=ea_blocks[:, :, 0, :, 3], in0=ea, scalar=ALPHA, in1=ea_blocks[:, :, 0, :, 0],
                                     op0=ALU.mult, op1=ALU.subtract).then_inc(ea_made, 1)
            low_part_x(0, 0)
            for h in range(2):
                dve.wait_ge(w1_hi_made, h + 1)
                dve.tensor_tensor(w1_lo[:, h * F // 2:(h + 1) * F // 2], w1[:, h * F // 2:(h + 1) * F // 2],
                                  w1_hi[:, h * F // 2:(h + 1) * F // 2], ALU.subtract).then_inc(w1_lo_made, 1)
            dve.wait_ge(eo_hi_made, 1)
            dve.scalar_tensor_tensor(out=fold_b[:, :, :, :], in0=eo_b_hi[:, :, :, :],
                                     scalar=minus_one_on(FOLD_B_LOW, slice(0, FOLD)), in1=eo_b_sb[:, :, :, :],
                                     op0=ALU.mult, op1=ALU.add).then_inc(fold_b_made, 1)
            blocks_b(0, 0)
            dve.wait_ge(zeroed, 3)
            blocks_low(0, 0)
            dve.wait_ge(wo_in, 16)
            dve.wait_ge(wo_product, 1)
            dve.scalar_tensor_tensor(out=wo_common[:, :, :].rearrange("p c d -> p (c d)"), in0=down_ps[0][:, :],
                                     scalar=ALPHA, in1=wo_sb[:, :, :].rearrange("p c d -> p (c d)"),
                                     op0=ALU.mult, op1=ALU.add).then_inc(wo_common_made, 1)
            fold_a_half(0)
            low_part_x(1, 1)
            blocks_b(1, 1)
            blocks_low(1, 1)
            dve.wait_ge(wo_common_made, 1)
            for n in range(FOLDS):
                if n == 2:
                    fold_a_half(1)
                add_w2(n)
            with dve.Fori(0, (GROUPS - 2) // 2) as i:
                group(i * 2 + 1, 1, i)
                group(i * 2 + 2, 0, i)
            finish(GROUPS // 2 - 1, 0)
            finish(GROUPS // 2 - 1, 1)

        @block.tensor
        def _(pe):
            def fold_w2(n):
                if n == 0:
                    pe.wait_ge(fold_b_made, 1)
                if n % (FOLDS // 2) == 0:
                    pe.wait_ge(fold_a_made, n // (FOLDS // 2) + 1)
                if n == 0:
                    pe.wait_ge(w1_made, 2)
                elif n == 2:
                    pe.wait_ge(wo_common_made, 1)
                elif n > 2:
                    pe.wait_ge(w2_made, n - 2)
                for k in range(2):
                    c, pair = n // 2, n % 2 * 2 + k
                    last = pe.matmul(w2_ps[n % 3][:, k * 2 * D:(k + 1) * 2 * D], fold_a[:, pair, c * 128:(c + 1) * 128],
                                     fold_b[:, pair, :, :].rearrange("p e d -> p (e d)"), start=True, stop=True)
                last.then_inc(w2_product, 1)

            def low(g, p, first=False):
                if not first:
                    pe.wait_ge(low_made, g * 2)
                pe.wait_ge(pair_a_made, (g + 1) * ROWS)
                pe.wait_ge(x_lo_made, g + 1)
                for q in range(PAIRS):
                    cols = slice(q * 2 * S, (q + 1) * 2 * S)
                    pe.matmul(low_ps[:, cols], pair_a[:, p, q, 0, :], x_hi[:, p, cols], start=True, stop=False)
                    last = pe.matmul(low_ps[:, cols], pair_a[:, p, q, 1, :], x_lo[:, p, cols], start=False, stop=True)
                last.then_inc(low_product, 1)

            def up_shared(g, p, c):
                cw = slice(c * 128, (c + 1) * 128)
                pe.wait_ge(hidden_made, g * CH - CH + c + 1)
                pe.matmul(up_ps[c][:, :], w1_hi[:, cw], x_hi[:, p, :], start=True, stop=False)
                pe.matmul(up_ps[c][:, :], w1_hi[:, cw], x_lo[:, p, :], start=False, stop=False)
                pe.matmul(up_ps[c][:, :], w1_lo[:, cw], x_hi[:, p, :], start=False, stop=False)

            def up_expert(g, p, c):
                if c == 0:
                    pe.wait_ge(low_made, g * 2 + 2)
                    pe.wait_ge(pair_b_made, (g + 1) * PAIRS)
                for q in range(PAIRS):
                    last = pe.matmul(up_ps[c][:, q * 2 * S:(q + 1) * 2 * S], pair_b[:, p, q, c * 128:(c + 1) * 128],
                                     low_blocks[:, p, q, :, :].rearrange("p h t -> p (h t)"),
                                     start=False, stop=(q == PAIRS - 1))
                last.then_inc(up_product, 1)

            def expert(g, r):
                return pe.value_load(ids_sb[0:1, bass.ds(g * ROWS + r, 1)], min_val=0, max_val=E - 1)

            def down(g, p, r, e):
                if r == 0:
                    pe.wait_ge(hidden_made, (g + 1) * CH)
                for c in range(CH):
                    last = pe.matmul(down_ps[p][:, r * D:(r + 1) * D], hidden[:, p, c, r * S:(r + 1) * S],
                                     w2[:, bass.ds(e, 1), c, :].rearrange("p e d -> p (e d)"),
                                     start=(c == 0), stop=(c == CH - 1))
                if r == ROWS - 1:
                    last.then_inc(down_product, 1)

            def group(g, p, prepare=True):
                experts = []
                for c in range(CH):
                    up_shared(g, p, c)
                    up_expert(g, p, c)
                    experts.append(expert(g - 1, c))
                if prepare:
                    low(g + 1, 1 - p)
                for r in range(ROWS):
                    down(g - 1, 1 - p, r, experts[r])

            pe.wait_ge(zeroed, 1)
            for n in range(WARM_UP):
                pe.matmul(up_ps[0][:, :], zeros[:, 0:128], zeros[:, :], start=True, stop=True)
            pe.wait_ge(common_in, 16)
            for h in range(2):
                pe.matmul(w1_ps[h][:, 0:F // 2], common_sb[:, C_IA:C_IB],
                          common_sb[:, C_IB + h * F // 2:C_IB + (h + 1) * F // 2], start=True, stop=True)\
                    .then_inc(w1_product, 1)
            pe.wait_ge(x_hi_made, 1)
            for c in range(CH):
                pe.wait_ge(w1_hi_made, c // 2 + 1)
                pe.matmul(up_ps[c][:, :], w1_hi[:, c * 128:(c + 1) * 128], x_hi[:, 0, :], start=True, stop=False)
            pe.wait_ge(x_lo_made, 1)
            for c in range(CH):
                pe.matmul(up_ps[c][:, :], w1_hi[:, c * 128:(c + 1) * 128], x_lo[:, 0, :], start=False, stop=False)
            for c in range(CH):
                pe.wait_ge(w1_lo_made, c // 2 + 1)
                pe.matmul(up_ps[c][:, :], w1_lo[:, c * 128:(c + 1) * 128], x_hi[:, 0, :], start=False, stop=False)
            low(0, 0, first=True)
            for c in range(CH):
                last = pe.matmul(down_ps[0][:, c * D:(c + 1) * D], common_sb[:, C_OA + c * 128:C_OA + (c + 1) * 128],
                                 common_sb[:, C_OB:C_END], start=True, stop=True)
            last.then_inc(wo_product, 1)
            for c in range(CH):
                up_expert(0, 0, c)
            low(1, 1)
            pe.wait_ge(ids_in, 16)
            folds = [(0, 1), (2, 3), (4, 5), (6, 7)]
            experts = []
            for c in range(CH):
                up_shared(1, 1, c)
                up_expert(1, 1, c)
                experts.append(expert(0, c))
                for n in folds[c]:
                    fold_w2(n)
            low(2, 0)
            pe.wait_ge(w2_made, FOLDS)
            for r in range(ROWS):
                down(0, 0, r, experts[r])
            with pe.Fori(0, (GROUPS - 4) // 2) as i:
                group(i * 2 + 2, 0)
                group(i * 2 + 3, 1)
            group(GROUPS - 2, 0)
            group(GROUPS - 1, 1, prepare=False)
            experts = [expert(GROUPS - 1, r) for r in range(ROWS)]
            pe.wait_ge(out_made, GROUPS - 2)
            for r in range(ROWS):
                down(GROUPS - 1, 1, r, experts[r])


def kernel(x, itok_B_0_7, L0_cond_wi, L0_cond_wo, L0_cond_common_wi_a, L0_cond_common_wi_b,
           L0_cond_common_wo_a, L0_cond_common_wo_b, L0_cond_experts_wi_a, L0_cond_experts_wi_b,
           L0_cond_experts_wo_a, L0_cond_experts_wo_b):
    import numpy as np
    import concourse.bacc as bacc
    from concourse.bass_utils import run_bass_kernel_spmd

    def lay(a):
        return np.ascontiguousarray(a)

    x = np.asarray(x)
    row = np.arange(128)
    masks = np.stack([np.where(row % n == k, -1.0, 0.0) for n, k in ((4, 1), (4, 2), (3, 1), (3, 2))], 1)
    masks = masks.astype(np.float32)
    ei_a = np.asarray(L0_cond_experts_wi_a).reshape(E * R, D)
    eo_a = np.asarray(L0_cond_experts_wo_a).reshape(EPAIRS, 2, R, F).transpose(1, 2, 0, 3)
    by_pair = np.asarray(L0_cond_experts_wo_b).reshape(EPAIRS, 2, D, R)
    eo_b = np.zeros((2, R, EPAIRS, 2, D), np.float32)
    for k in range(2):
        eo_b[k, :, :, k, :] = by_pair[:, k].transpose(2, 0, 1)
    arrays = {
        "x_t": lay(x.reshape(B * S, D).T).reshape(D, GROUPS, TOK),
        "x": lay(x.reshape(GROUPS // 2, 2, ROWS, S, D).transpose(3, 1, 0, 2, 4)),
        "ids": lay(np.asarray(itok_B_0_7).reshape(1, B)),
        "packed": lay(np.concatenate([np.asarray(L0_cond_wi).T, ei_a.T, masks], 1)),
        "common": lay(np.concatenate([np.asarray(L0_cond_common_wi_a), np.asarray(L0_cond_common_wi_b).T,
                                      np.asarray(L0_cond_common_wo_a), np.asarray(L0_cond_common_wo_b).T], 1)),
        "ei_b": lay(np.asarray(L0_cond_experts_wi_b).transpose(0, 2, 1)),
        "eo_a": lay(eo_a.reshape(2 * R, EPAIRS, F)),
        "eo_b": eo_b.reshape(2 * R, EPAIRS, 2, D),
        "wo_t": lay(np.asarray(L0_cond_wo).T.reshape(CH, 128, D).transpose(1, 0, 2)),
    }
    nc = bacc.Bacc("TRN2", target_bir_lowering=False, num_devices=1)
    args = [nc.dram_tensor(n, a.shape, mybir.dt.from_np(a.dtype), kind="ExternalInput").ap()
            for n, a in arrays.items()]
    args.append(nc.dram_tensor("out", (S, GROUPS, ROWS, D), mybir.dt.float32, kind="ExternalOutput").ap())
    build(nc, *args)
    result = run_bass_kernel_spmd(nc, [arrays], core_ids=[0])
    return lay(result.results[0]["out"].reshape(S, B, D).transpose(1, 0, 2))
```

```python
import concourse.bass as bass
import concourse.mybir as mybir

B, S, D, F, R, E = 32, 128, 128, 512, 16, 8
ALPHA = 2.0
CH = F // 128
HALF = E // 2
STACK = (HALF + 2) * R
UNSPLIT = 1
UP_AHEAD = 8
SLOTS = 4
OUT_PAIRS = B // 2
EPAIRS = E // 2
FOLD = 3 * 2 * R
FOLDS = 2 * CH
WARM_UP = 6


def build(nc, x_t, x, ids, wi_t, up_factors, co, eo_a, eo_b, wo_t, out):
    F32, F32R, I32 = mybir.dt.float32, mybir.dt.float32r, mybir.dt.int32
    ALU, ACT = mybir.AluOpType, mybir.ActivationFunctionType

    from contextlib import ExitStack
    ctx = ExitStack()
    with ctx:
        def sb(name, shape, dt):
            return ctx.enter_context(nc.sbuf_tensor(name, shape, dt))

        def bank(name):
            return ctx.enter_context(nc.psum_tensor(name, [128, 512], F32))

        def sem(name):
            return ctx.enter_context(nc.semaphore(name))

        ids_sb = sb("ids_sb", [1, B], I32)
        xt_sb = sb("xt_sb", [128, B, S], F32)
        x_sb = sb("x_sb", [128, B, D], F32)
        wi_sb = sb("wi_sb", [128, F], F32)
        up_sb = sb("up_sb", [STACK, 2, F + HALF * D], F32)
        up_b_hi = sb("up_b_hi", [STACK, 2, F], F32R)
        up_b_lo = sb("up_b_lo", [STACK, 2, F], F32R)
        up_a_hi = sb("up_a_hi", [STACK, 2, HALF, D], F32R)
        up_a_lo = sb("up_a_lo", [STACK, 2, HALF, D], F32R)
        co_sb = sb("co_sb", [R, F + D], F32)
        eo_a_sb = sb("eo_a_sb", [FOLD, EPAIRS, F], F32)
        eo_b_sb = sb("eo_b_sb", [FOLD, EPAIRS, 2, D], F32)
        wo_sb = sb("wo_sb", [128, CH, D], F32)

        w1 = sb("w1", [128, E, F], F32)
        w2 = sb("w2", [128, E, CH, D], F32)
        wo_common = sb("wo_common", [128, CH, D], F32)
        fold_a = sb("fold_a", [FOLD, EPAIRS, F], F32R)
        fold_b = sb("fold_b", [FOLD, EPAIRS, 2, D], F32R)
        row_w1 = sb("row_w1", [128, SLOTS, F], F32)
        zeros = sb("zeros", [128, 512], F32R)

        hidden = sb("hidden", [128, UP_AHEAD, CH, S], F32)
        out_sb = sb("out_sb", [128, 2, 2, D], F32)

        up_ps = [bank(f"up_ps{k}") for k in range(SLOTS)]
        down_ps = [bank(f"down_ps{p}") for p in range(2)]
        w2_ps = [bank(f"w2_ps{k}") for k in range(2)] + [down_ps[1]]

        ids_in, wi_in, co_in, wo_in = sem("ids_in"), sem("wi_in"), sem("co_in"), sem("wo_in")
        up_b_in = [sem(f"up_b_in{h}") for h in range(2)]
        up_a_in = [sem(f"up_a_in{h}") for h in range(2)]
        eo_a_in, eo_b_in = sem("eo_a_in"), sem("eo_b_in")
        xt_first_in, xt_rest_in = sem("xt_first_in"), sem("xt_rest_in")
        x_first_in, x_rest_in = sem("x_first_in"), sem("x_rest_in")
        w1_product = sem("w1_product")
        wo_product = sem("wo_product")
        w2_product = sem("w2_product")
        up_product = sem("up_product")
        down_product = sem("down_product")
        fold_a_rounded, fold_b_rounded = sem("fold_a_rounded"), sem("fold_b_rounded")
        first_w1_made = sem("first_w1_made")
        hidden_made = sem("hidden_made")
        up_hi_made, up_lo_made = sem("up_hi_made"), sem("up_lo_made")
        w1_made = sem("w1_made")
        wo_common_made = sem("wo_common_made")
        w2_made = sem("w2_made")
        row_w1_made = sem("row_w1_made")
        out_made = sem("out_made")
        zeroed, fold_a_made, fold_b_made = sem("zeroed"), sem("fold_a_made"), sem("fold_b_made")
        stored = [sem(f"stored{p}") for p in range(2)]

        up_b = up_sb[:, :, 0:F]
        up_a = up_sb[:, :, F:F + HALF * D].rearrange("p h (e d) -> p h e d", e=HALF)

        block = ctx.enter_context(nc.Block())

        @block.sync
        def _(sp):
            first_cols = F + UNSPLIT * D
            sp.dma_start(up_sb[:, 0, 0:first_cols], up_factors[0, :, 0:first_cols]).then_inc(up_b_in[0], 16)
            sp.dma_start(up_sb[:, 1, 0:F], up_factors[1, :, 0:F]).then_inc(up_b_in[1], 16)
            sp.dma_start(wi_sb[:, :], wi_t).then_inc(wi_in, 16)
            sp.dma_start(eo_b_sb[:, :, :, :].rearrange("p a e d -> p (a e d)"),
                         bass.AP(eo_b.tensor, 0, [[0, 3], [EPAIRS * 2 * D, 2 * R], [1, EPAIRS * 2 * D]]))\
                .then_inc(eo_b_in, 16)
            sp.dma_start(eo_a_sb[:, :, :].rearrange("p a f -> p (a f)"),
                         bass.AP(eo_a.tensor, 0, [[0, 3], [EPAIRS * F, 2 * R], [1, EPAIRS * F]]))\
                .then_inc(eo_a_in, 16)
            sp.dma_start(xt_sb[:, 0:UP_AHEAD, :], x_t[:, 0:UP_AHEAD, :]).then_inc(xt_first_in, 16)
            sp.dma_start(wo_sb[:, :, :], wo_t).then_inc(wo_in, 16)
            sp.dma_start(x_sb[:, 0:UP_AHEAD, :], x[:, 0:UP_AHEAD, :]).then_inc(x_first_in, 16)
            sp.dma_start(xt_sb[:, UP_AHEAD:B, :], x_t[:, UP_AHEAD:B, :]).then_inc(xt_rest_in, 16)
            sp.dma_start(x_sb[:, UP_AHEAD:B, :], x[:, UP_AHEAD:B, :]).then_inc(x_rest_in, 16)

            def store(n, p):
                sp.wait_ge(out_made, n + 1)
                sp.dma_start(out[:, bass.ds(n, 1), :, :].rearrange("t n r d -> t (n r) d"),
                             out_sb[:, p, :, :]).then_inc(stored[p], 16)

            with sp.Fori(0, OUT_PAIRS // 2 - 1) as i:
                for p in range(2):
                    store(i * 2 + p, p)
            store(OUT_PAIRS - 2, 0)
            for r in range(2):
                sp.wait_ge(out_made, OUT_PAIRS + r)
                sp.dma_start(out[:, OUT_PAIRS - 1, r, :], out_sb[:, 1, r, :]).then_inc(stored[1], 16)
            for p in range(2):
                sp.wait_ge(stored[p], 16 * (OUT_PAIRS // 2 + p))

        @block.gpsimd
        def _(pool):
            pool.memset(zeros[:, :].bitcast(F32), 0.0).then_inc(zeroed, 1)

            low = slice(2 * 2 * R, 3 * 2 * R)
            pool.wait_ge(zeroed, 1)
            pool.wait_ge(fold_b_rounded, 1)
            pool.tensor_tensor(fold_b[low, :, :, :].rearrange("p a e d -> p (a e d)"),
                               eo_b_sb[low, :, :, :].rearrange("p a e d -> p (a e d)"),
                               fold_b[low, :, :, :].rearrange("p a e d -> p (a e d)"), ALU.subtract)\
                .then_inc(fold_b_made, 1)
            low = slice(2 * R, 2 * 2 * R)
            pool.wait_ge(fold_b_made, 1)
            for c in range(CH):
                cols = slice(c * 128, (c + 1) * 128)
                pool.wait_ge(fold_a_rounded, c // 2 + 1)
                pool.tensor_tensor(fold_a[low, :, cols], eo_a_sb[low, :, cols], fold_a[low, :, cols], ALU.subtract)\
                    .then_inc(fold_a_made, 1)

        @block.scalar
        def _(act):
            first_cols = F + UNSPLIT * D
            act.dma_start(up_sb[:, 0, first_cols:], up_factors[0, :, first_cols:]).then_inc(up_a_in[0], 16)
            act.dma_start(up_sb[:, 1, F:], up_factors[1, :, F:]).then_inc(up_a_in[1], 16)
            act.dma_start(ids_sb[:, :], ids).then_inc(ids_in, 16)
            act.dma_start(co_sb[:, :], co).then_inc(co_in, 16)

            def expert(j):
                return act.value_load(ids_sb[0:1, j:j + 1], min_val=0, max_val=E - 1)

            act.wait_ge(eo_b_in, 16)
            act.activation(fold_b[:, :, :, :].rearrange("p a e d -> p (a e d)"),
                           eo_b_sb[:, :, :, :].rearrange("p a e d -> p (a e d)"), ACT.Copy).then_inc(fold_b_rounded, 1)
            act.wait_ge(ids_in, 16)
            experts = [expert(j) for j in range(SLOTS)]
            act.wait_ge(eo_a_in, 16)
            for h in range(2):
                cols = slice(h * F // 2, (h + 1) * F // 2)
                act.activation(fold_a[:, :, cols], eo_a_sb[:, :, cols], ACT.Copy).then_inc(fold_a_rounded, 1)

            def copy_w1(j, e):
                act.wait_ge(w1_made, e + 1)
                if j >= SLOTS:
                    act.wait_ge(up_product, j - SLOTS + 1)
                act.activation(row_w1[:, j % SLOTS, :], w1[:, bass.ds(e, 1), :].rearrange("p e f -> p (e f)"),
                               ACT.Copy).then_inc(first_w1_made, 1)

            def relu(j, k):
                act.wait_ge(up_product, j + 1)
                act.activation(hidden[:, k, :, :].rearrange("p c t -> p (c t)"), up_ps[k % SLOTS][:, :],
                               ACT.Relu).then_inc(hidden_made, 1)

            for j in range(SLOTS):
                copy_w1(j, experts[j])
            experts += [expert(j) for j in range(SLOTS, UP_AHEAD)]
            for j in range(UP_AHEAD):
                relu(j, j)
                if j + SLOTS < UP_AHEAD:
                    copy_w1(j + SLOTS, experts[j + SLOTS])
            with act.Fori(1, B // UP_AHEAD) as i:
                for k in range(UP_AHEAD):
                    relu(i * UP_AHEAD + k, k)

        @block.vector
        def _(dve):
            def finish(n, p, reused=True):
                if reused:
                    dve.wait_ge(stored[p], (n - p) * 8)
                dve.wait_ge(down_product, n * 2 + 2)
                dve.tensor_tensor(out_sb[:, p, :, :], down_ps[p][:, 0:2 * D].rearrange("p (r d) -> p r d", r=2),
                                  x_sb[:, bass.ds(n * 2, 2), :], ALU.add).then_inc(out_made, 1)

            def copy_w1(j, k):
                e = dve.value_load(ids_sb[0:1, bass.ds(j, 1)], min_val=0, max_val=E - 1)
                dve.wait_ge(up_product, j - SLOTS + 1)
                dve.tensor_copy(row_w1[:, k, :], w1[:, bass.ds(e, 1), :].rearrange("p e f -> p (e f)"))\
                    .then_inc(row_w1_made, 1)

            for h in range(2):
                to_split = slice(UNSPLIT if h == 0 else 0, HALF)
                parts = ((up_b_in[h], up_b[:, h, :], up_b_hi[:, h, :], up_b_lo[:, h, :]),
                         (up_a_in[h], up_a[:, h, to_split, :], up_a_hi[:, h, to_split, :], up_a_lo[:, h, to_split, :]))
                for loaded, whole, high, low in parts:
                    dve.wait_ge(loaded, 16)
                    dve.tensor_copy(high, whole).then_inc(up_hi_made, 1)
                for k, (loaded, whole, high, low) in enumerate(parts):
                    dve.wait_ge(up_hi_made, h * 2 + k + 1)
                    dve.tensor_tensor(low, whole, high, ALU.subtract).then_inc(up_lo_made, 1)
            dve.wait_ge(wi_in, 16)
            for e in range(E):
                dve.wait_ge(w1_product, e + 1)
                dve.scalar_tensor_tensor(out=w1[:, e, :], in0=up_ps[e % SLOTS][:, :], scalar=ALPHA, in1=wi_sb[:, :],
                                         op0=ALU.mult, op1=ALU.add).then_inc(w1_made, 1)
            dve.wait_ge(wo_in, 16)
            dve.wait_ge(wo_product, 1)
            dve.scalar_tensor_tensor(out=wo_common[:, :, :].rearrange("p c d -> p (c d)"), in0=down_ps[0][:, :],
                                     scalar=ALPHA, in1=wo_sb[:, :, :].rearrange("p c d -> p (c d)"),
                                     op0=ALU.mult, op1=ALU.add).then_inc(wo_common_made, 1)
            dve.wait_ge(wo_common_made, 1)
            for n in range(FOLDS):
                c, e = n // 2, n % 2 * 4
                dve.wait_ge(w2_product, n + 1)
                dve.scalar_tensor_tensor(
                    out=w2[:, e:e + 4, c, :], in0=w2_ps[n % 3][:, :].rearrange("p (e d) -> p e d", e=4), scalar=ALPHA,
                    in1=wo_common[:, c, :].rearrange("p (o d) -> p o d", o=1).to_broadcast([128, 4, D]),
                    op0=ALU.mult, op1=ALU.add).then_inc(w2_made, 1)
            for k in range(SLOTS):
                copy_w1(UP_AHEAD + k, k)
            dve.wait_ge(x_first_in, 16)
            for n in range(2):
                finish(n, n, reused=False)
            dve.wait_ge(x_rest_in, 16)
            with dve.Fori(UP_AHEAD // SLOTS + 1, B // SLOTS) as i:
                for k in range(SLOTS):
                    if k % 2 == 0:
                        finish(i * 2 + (k // 2 - 4), k // 2)
                    copy_w1(i * SLOTS + k, k)
            for n in range(OUT_PAIRS - 4, OUT_PAIRS - 1):
                finish(n, n % 2)
            dve.wait_ge(stored[1], (OUT_PAIRS - 2) * 8)
            for r, bank_of_row in ((0, down_ps[1]), (1, w2_ps[0])):
                dve.wait_ge(down_product, B - 1 + r)
                dve.tensor_tensor(out_sb[:, 1, r, :], bank_of_row[:, 0:D], x_sb[:, B - 2 + r, :], ALU.add)\
                    .then_inc(out_made, 1)

        @block.tensor
        def _(pe):
            def expert(j):
                return pe.value_load(ids_sb[0:1, bass.ds(j, 1)], min_val=0, max_val=E - 1)

            def up(j, k, first=False):
                if first:
                    pe.wait_ge(first_w1_made, j + 1)
                else:
                    pe.wait_ge(row_w1_made, j - UP_AHEAD + 1)
                if first and j < SLOTS:
                    pe.wait_ge(w1_made, E - SLOTS + j + 1)
                else:
                    pe.wait_ge(hidden_made, j - SLOTS + 1)
                for c in range(CH):
                    last = pe.matmul(up_ps[k][:, c * S:(c + 1) * S],
                                     row_w1[:, k, c * 128:(c + 1) * 128],
                                     xt_sb[:, bass.ds(j, 1), :].rearrange("p j t -> p (j t)"), start=True, stop=True)
                last.then_inc(up_product, 1)

            def down(j, k, e, out_read=None, into=None):
                if into is None:
                    into = down_ps[k // 2 % 2][:, k % 2 * D:(k % 2 + 1) * D]
                if out_read is not None:
                    pe.wait_ge(out_made, out_read)
                pe.wait_ge(hidden_made, j + 1)
                for c in range(CH):
                    last = pe.matmul(into, hidden[:, k, c, :],
                                     w2[:, bass.ds(e, 1), c, :].rearrange("p e d -> p (e d)"),
                                     start=(c == 0), stop=(c == CH - 1))
                last.then_inc(down_product, 1)

            def fold_w2(n):
                if n == 0:
                    pe.wait_ge(fold_b_made, 1)
                if n % 2 == 0:
                    pe.wait_ge(fold_a_made, n // 2 + 1)
                if n >= 3:
                    pe.wait_ge(w2_made, n - 2)
                for k in range(2):
                    c, pair = n // 2, n % 2 * 2 + k
                    last = pe.matmul(w2_ps[n % 3][:, k * 2 * D:(k + 1) * 2 * D], fold_a[:, pair, c * 128:(c + 1) * 128],
                                     fold_b[:, pair, :, :].rearrange("p e d -> p (e d)"), start=True, stop=True)
                last.then_inc(w2_product, 1)

            pe.wait_ge(zeroed, 1)
            for n in range(WARM_UP):
                pe.matmul(down_ps[0][:, :], zeros[:, 0:128], zeros[:, :], start=True, stop=True)
            for e in range(E):
                h = e // HALF
                if e == 0:
                    pe.wait_ge(up_b_in[0], 16)
                if e >= SLOTS:
                    pe.wait_ge(w1_made, e - SLOTS + 1)
                if e < UNSPLIT:
                    last = pe.matmul(up_ps[e % SLOTS][:, :], up_a[:, h, e % HALF, :], up_b[:, h, :],
                                     start=True, stop=True)
                else:
                    if e == UNSPLIT or e == HALF:
                        pe.wait_ge(up_lo_made, h * 2 + 2)
                    for n, (a, b) in enumerate(((up_a_hi, up_b_hi), (up_a_lo, up_b_hi), (up_a_hi, up_b_lo))):
                        last = pe.matmul(up_ps[e % SLOTS][:, :], a[:, h, e % HALF, :], b[:, h, :],
                                         start=(n == 0), stop=(n == 2))
                last.then_inc(w1_product, 1)
            pe.wait_ge(co_in, 16)
            for c in range(CH):
                last = pe.matmul(down_ps[0][:, c * D:(c + 1) * D], co_sb[:, c * 128:(c + 1) * 128],
                                 co_sb[:, F:F + D], start=True, stop=True)
            last.then_inc(wo_product, 1)
            for n in range(2):
                fold_w2(n)
            pe.wait_ge(ids_in, 16)
            pe.wait_ge(xt_first_in, 16)
            experts = []
            for j in range(UP_AHEAD):
                up(j, j % SLOTS, first=True)
                experts.append(expert(j))
                if j + 2 < FOLDS:
                    fold_w2(j + 2)
            pe.wait_ge(w2_made, FOLDS)
            pe.wait_ge(wo_common_made, 1)
            for j in range(UP_AHEAD - 1):
                down(j, j, experts[j], out_read=(j // 2 - 1 if j >= 4 and j % 2 == 0 else None))
            pe.wait_ge(xt_rest_in, 16)
            with pe.Fori(1, B // UP_AHEAD) as i:
                for k in range(UP_AHEAD):
                    j = i * UP_AHEAD + k
                    up(j, k % SLOTS)
                    down(j - 1, (k - 1) % UP_AHEAD, expert(j - 1),
                         out_read=(i * (UP_AHEAD // 2) + (k // 2 - 1) if k % 2 == 1 else None))
            down(B - 1, UP_AHEAD - 1, expert(B - 1), into=w2_ps[0][:, 0:D])


def kernel(x, itok_B_0_7, L0_cond_wi, L0_cond_wo, L0_cond_common_wi_a, L0_cond_common_wi_b,
           L0_cond_common_wo_a, L0_cond_common_wo_b, L0_cond_experts_wi_a, L0_cond_experts_wi_b,
           L0_cond_experts_wo_a, L0_cond_experts_wo_b):
    import numpy as np
    import concourse.bacc as bacc
    from concourse.bass_utils import run_bass_kernel_spmd

    def lay(a):
        return np.ascontiguousarray(a)

    x = np.asarray(x)
    ei_a = np.asarray(L0_cond_experts_wi_a)
    up_factors = np.zeros((2, STACK, F + HALF * D), np.float32)
    for h in range(2):
        up_factors[h, :HALF * R, :F] = np.asarray(L0_cond_experts_wi_b)[h * HALF:(h + 1) * HALF]\
            .transpose(0, 2, 1).reshape(HALF * R, F)
        up_factors[h, HALF * R:(HALF + 1) * R, :F] = np.asarray(L0_cond_common_wi_b).T
        for k in range(HALF):
            cols = slice(F + k * D, F + (k + 1) * D)
            up_factors[h, k * R:(k + 1) * R, cols] = ei_a[h * HALF + k]
            up_factors[h, HALF * R:(HALF + 1) * R, cols] = np.asarray(L0_cond_common_wi_a)
    eo_a = np.asarray(L0_cond_experts_wo_a).reshape(EPAIRS, 2, R, F).transpose(1, 2, 0, 3)
    by_pair = np.asarray(L0_cond_experts_wo_b).reshape(EPAIRS, 2, D, R)
    eo_b = np.zeros((2, R, EPAIRS, 2, D), np.float32)
    for k in range(2):
        eo_b[k, :, :, k, :] = by_pair[:, k].transpose(2, 0, 1)
    arrays = {
        "x_t": lay(x.transpose(2, 0, 1)),
        "x": lay(x.transpose(1, 0, 2)),
        "ids": lay(np.asarray(itok_B_0_7).reshape(1, B)),
        "wi_t": lay(np.asarray(L0_cond_wi).T),
        "up_factors": up_factors,
        "co": lay(np.concatenate([np.asarray(L0_cond_common_wo_a), np.asarray(L0_cond_common_wo_b).T], 1)),
        "eo_a": lay(eo_a.reshape(2 * R, EPAIRS, F)),
        "eo_b": eo_b.reshape(2 * R, EPAIRS, 2, D),
        "wo_t": lay(np.asarray(L0_cond_wo).T.reshape(CH, 128, D).transpose(1, 0, 2)),
    }
    nc = bacc.Bacc("TRN2", target_bir_lowering=False, num_devices=1)
    args = [nc.dram_tensor(n, a.shape, mybir.dt.from_np(a.dtype), kind="ExternalInput").ap()
            for n, a in arrays.items()]
    args.append(nc.dram_tensor("out", (S, OUT_PAIRS, 2, D), mybir.dt.float32, kind="ExternalOutput").ap())
    build(nc, *args)
    result = run_bass_kernel_spmd(nc, [arrays], core_ids=[0])
    return lay(result.results[0]["out"].reshape(S, B, D).transpose(1, 0, 2))
```
